# Optimizing a Trainium2 kernel written in Bass

```python
import numpy as np
import jax
import jax.numpy as jnp

def _softmax(x, axis=-1):
    return jax.nn.softmax(x, axis=axis)

def _gelu(x):
    return jax.nn.gelu(x, approximate=True)

def _silu(x):
    return jax.nn.silu(x)

def _sigmoid(x):
    return jax.nn.sigmoid(x)

def _layernorm(x, axis=-1, eps=1e-05):
    m = jnp.mean(x, axis=axis, keepdims=True)
    v = jnp.var(x, axis=axis, keepdims=True)
    return (x - m) / jnp.sqrt(v + eps)

def _scatter_add(tgt, idx, src, axis=0):
    return tgt.at[idx].add(src)

def _segment_sum(src, seg, n):
    return jax.ops.segment_sum(src, seg, n)
kernel_name = 'mk_dlrm_tower_d1_rec_r8_cec4bd'

def setup_inputs(seed: int=0):
    np.random.seed(seed)
    _w = jnp.asarray

    def _rec_inputs():
        import jax
        import jax.numpy as jnp
        _tk = jax.random.key(seed)
        dense_ctx = jax.random.normal(jax.random.fold_in(_tk, 190), (2048, 16), jnp.float32)
        ids = jnp.stack([jax.random.randint(jax.random.fold_in(_tk, 200 + f), (2048,), 0, v, jnp.int32) for f, v in enumerate([1000, 12500, 1000, 1000, 1250, 12500, 125000, 1000, 1250, 12500, 1000, 1000, 1250, 1000, 12500, 12500, 1000, 1000, 12500, 1000, 1000, 1000, 1000, 1000, 1000, 12500, 12500, 12500, 1000, 1000, 1000, 1000])], axis=1)
        tbl_0 = 0.05 * jax.random.normal(jax.random.fold_in(_tk, 500 + 0), (1000, 128), jnp.float32)
        tbl_1 = 0.05 * jax.random.normal(jax.random.fold_in(_tk, 500 + 1), (12500, 128), jnp.float32)
        tbl_2 = 0.05 * jax.random.normal(jax.random.fold_in(_tk, 500 + 2), (1000, 128), jnp.float32)
        tbl_3 = 0.05 * jax.random.normal(jax.random.fold_in(_tk, 500 + 3), (1000, 128), jnp.float32)
        tbl_4 = 0.05 * jax.random.normal(jax.random.fold_in(_tk, 500 + 4), (1250, 128), jnp.float32)
        tbl_5 = 0.05 * jax.random.normal(jax.random.fold_in(_tk, 500 + 5), (12500, 128), jnp.float32)
        tbl_6 = 0.05 * jax.random.normal(jax.random.fold_in(_tk, 500 + 6), (125000, 128), jnp.float32)
        tbl_7 = 0.05 * jax.random.normal(jax.random.fold_in(_tk, 500 + 7), (1000, 128), jnp.float32)
        tbl_8 = 0.05 * jax.random.normal(jax.random.fold_in(_tk, 500 + 8), (1250, 128), jnp.float32)
        tbl_9 = 0.05 * jax.random.normal(jax.random.fold_in(_tk, 500 + 9), (12500, 128), jnp.float32)
        tbl_10 = 0.05 * jax.random.normal(jax.random.fold_in(_tk, 500 + 10), (1000, 128), jnp.float32)
        tbl_11 = 0.05 * jax.random.normal(jax.random.fold_in(_tk, 500 + 11), (1000, 128), jnp.float32)
        tbl_12 = 0.05 * jax.random.normal(jax.random.fold_in(_tk, 500 + 12), (1250, 128), jnp.float32)
        tbl_13 = 0.05 * jax.random.normal(jax.random.fold_in(_tk, 500 + 13), (1000, 128), jnp.float32)
        tbl_14 = 0.05 * jax.random.normal(jax.random.fold_in(_tk, 500 + 14), (12500, 128), jnp.float32)
        tbl_15 = 0.05 * jax.random.normal(jax.random.fold_in(_tk, 500 + 15), (12500, 128), jnp.float32)
        tbl_16 = 0.05 * jax.random.normal(jax.random.fold_in(_tk, 500 + 16), (1000, 128), jnp.float32)
        tbl_17 = 0.05 * jax.random.normal(jax.random.fold_in(_tk, 500 + 17), (1000, 128), jnp.float32)
        tbl_18 = 0.05 * jax.random.normal(jax.random.fold_in(_tk, 500 + 18), (12500, 128), jnp.float32)
        tbl_19 = 0.05 * jax.random.normal(jax.random.fold_in(_tk, 500 + 19), (1000, 128), jnp.float32)
        tbl_20 = 0.05 * jax.random.normal(jax.random.fold_in(_tk, 500 + 20), (1000, 128), jnp.float32)
        tbl_21 = 0.05 * jax.random.normal(jax.random.fold_in(_tk, 500 + 21), (1000, 128), jnp.float32)
        tbl_22 = 0.05 * jax.random.normal(jax.random.fold_in(_tk, 500 + 22), (1000, 128), jnp.float32)
        tbl_23 = 0.05 * jax.random.normal(jax.random.fold_in(_tk, 500 + 23), (1000, 128), jnp.float32)
        tbl_24 = 0.05 * jax.random.normal(jax.random.fold_in(_tk, 500 + 24), (1000, 128), jnp.float32)
        tbl_25 = 0.05 * jax.random.normal(jax.random.fold_in(_tk, 500 + 25), (12500, 128), jnp.float32)
        tbl_26 = 0.05 * jax.random.normal(jax.random.fold_in(_tk, 500 + 26), (12500, 128), jnp.float32)
        tbl_27 = 0.05 * jax.random.normal(jax.random.fold_in(_tk, 500 + 27), (12500, 128), jnp.float32)
        tbl_28 = 0.05 * jax.random.normal(jax.random.fold_in(_tk, 500 + 28), (1000, 128), jnp.float32)
        tbl_29 = 0.05 * jax.random.normal(jax.random.fold_in(_tk, 500 + 29), (1000, 128), jnp.float32)
        tbl_30 = 0.05 * jax.random.normal(jax.random.fold_in(_tk, 500 + 30), (1000, 128), jnp.float32)
        tbl_31 = 0.05 * jax.random.normal(jax.random.fold_in(_tk, 500 + 31), (1000, 128), jnp.float32)
        _rk = jax.random.fold_in(_tk, 7)
        W_top1 = 0.0441942 * jax.random.normal(jax.random.fold_in(_tk, 801), (512, 512), jnp.float32)
        W_top2 = 0.0441942 * jax.random.normal(jax.random.fold_in(_tk, 802), (512, 256), jnp.float32)
        W_top3 = 0.0625 * jax.random.normal(jax.random.fold_in(_tk, 803), (256, 1), jnp.float32)
        b_top1 = jnp.zeros((512,), jnp.float32)
        b_top2 = jnp.zeros((256,), jnp.float32)
        return (dense_ctx, ids, tbl_0, tbl_1, tbl_2, tbl_3, tbl_4, tbl_5, tbl_6, tbl_7, tbl_8, tbl_9, tbl_10, tbl_11, tbl_12, tbl_13, tbl_14, tbl_15, tbl_16, tbl_17, tbl_18, tbl_19, tbl_20, tbl_21, tbl_22, tbl_23, tbl_24, tbl_25, tbl_26, tbl_27, tbl_28, tbl_29, tbl_30, tbl_31, W_top1, b_top1, W_top2, b_top2, W_top3)
    dense_ctx, ids, tbl_0, tbl_1, tbl_2, tbl_3, tbl_4, tbl_5, tbl_6, tbl_7, tbl_8, tbl_9, tbl_10, tbl_11, tbl_12, tbl_13, tbl_14, tbl_15, tbl_16, tbl_17, tbl_18, tbl_19, tbl_20, tbl_21, tbl_22, tbl_23, tbl_24, tbl_25, tbl_26, tbl_27, tbl_28, tbl_29, tbl_30, tbl_31, W_top1, b_top1, W_top2, b_top2, W_top3 = _rec_inputs()

    def _L0_rec_setup():
        import jax, jax.numpy as jnp
        import numpy as np
        B, F, D = (2048, 32, 128)
        key = jax.random.key(seed)
        inputs = jax.random.normal(key, (B, F, D), dtype=jnp.float32)
        return {'inputs': inputs}
    _L0_rec_all = _L0_rec_setup()
    _L0_rec_in = {k: v for k, v in _L0_rec_all.items() if k in ()}
    del _L0_rec_all
    return {'dense_ctx': dense_ctx, 'ids': ids, 'tbl_0': tbl_0, 'tbl_1': tbl_1, 'tbl_2': tbl_2, 'tbl_3': tbl_3, 'tbl_4': tbl_4, 'tbl_5': tbl_5, 'tbl_6': tbl_6, 'tbl_7': tbl_7, 'tbl_8': tbl_8, 'tbl_9': tbl_9, 'tbl_10': tbl_10, 'tbl_11': tbl_11, 'tbl_12': tbl_12, 'tbl_13': tbl_13, 'tbl_14': tbl_14, 'tbl_15': tbl_15, 'tbl_16': tbl_16, 'tbl_17': tbl_17, 'tbl_18': tbl_18, 'tbl_19': tbl_19, 'tbl_20': tbl_20, 'tbl_21': tbl_21, 'tbl_22': tbl_22, 'tbl_23': tbl_23, 'tbl_24': tbl_24, 'tbl_25': tbl_25, 'tbl_26': tbl_26, 'tbl_27': tbl_27, 'tbl_28': tbl_28, 'tbl_29': tbl_29, 'tbl_30': tbl_30, 'tbl_31': tbl_31, 'W_top1': W_top1, 'b_top1': b_top1, 'W_top2': W_top2, 'b_top2': b_top2, 'W_top3': W_top3}

def reference(dense_ctx, ids, tbl_0, tbl_1, tbl_2, tbl_3, tbl_4, tbl_5, tbl_6, tbl_7, tbl_8, tbl_9, tbl_10, tbl_11, tbl_12, tbl_13, tbl_14, tbl_15, tbl_16, tbl_17, tbl_18, tbl_19, tbl_20, tbl_21, tbl_22, tbl_23, tbl_24, tbl_25, tbl_26, tbl_27, tbl_28, tbl_29, tbl_30, tbl_31, W_top1, b_top1, W_top2, b_top2, W_top3):
    import jax
    import jax.numpy as jnp

    def _L0_rec_ref(inputs):
        import jax, jax.numpy as jnp
        import numpy as np
        B, F, D = (2048, 32, 128)
        dot_products = jnp.einsum('bfd,bgd->bfg', inputs, inputs)
        num_feas = inputs.shape[1]
        iu, ju = jnp.triu_indices(num_feas, k=1)
        return dot_products[:, iu, ju]
    e = jnp.stack([tbl_0[ids[:, 0]], tbl_1[ids[:, 1]], tbl_2[ids[:, 2]], tbl_3[ids[:, 3]], tbl_4[ids[:, 4]], tbl_5[ids[:, 5]], tbl_6[ids[:, 6]], tbl_7[ids[:, 7]], tbl_8[ids[:, 8]], tbl_9[ids[:, 9]], tbl_10[ids[:, 10]], tbl_11[ids[:, 11]], tbl_12[ids[:, 12]], tbl_13[ids[:, 13]], tbl_14[ids[:, 14]], tbl_15[ids[:, 15]], tbl_16[ids[:, 16]], tbl_17[ids[:, 17]], tbl_18[ids[:, 18]], tbl_19[ids[:, 19]], tbl_20[ids[:, 20]], tbl_21[ids[:, 21]], tbl_22[ids[:, 22]], tbl_23[ids[:, 23]], tbl_24[ids[:, 24]], tbl_25[ids[:, 25]], tbl_26[ids[:, 26]], tbl_27[ids[:, 27]], tbl_28[ids[:, 28]], tbl_29[ids[:, 29]], tbl_30[ids[:, 30]], tbl_31[ids[:, 31]]], axis=1)
    z = _L0_rec_ref(e)
    z = z.reshape(z.shape[0], -1)
    h = jnp.concatenate([z, dense_ctx], axis=1)
    h = jnp.maximum(h @ W_top1 + b_top1, 0.0)
    h = jnp.maximum(h @ W_top2 + b_top2, 0.0)
    y = h @ W_top3
    return y

_drawn_inputs = setup_inputs


def setup_inputs(seed=0):
    import zlib

    import numpy as np

    out = dict(_drawn_inputs(seed))
    spreads = {'b_top1': (0.0, 0.1), 'b_top2': (0.0, 0.1)}
    factors = {}
    for name, (base, spread) in spreads.items():
        noise = np.random.default_rng([zlib.crc32(name.encode()), seed]).standard_normal(out[name].shape)
        drawn = base * np.exp(spread * noise) if base else spread * noise
        out[name] = jnp.asarray(drawn.astype(out[name].dtype))
    for name, factor in factors.items():
        out[name] = (out[name] * factor).astype(out[name].dtype)
    return out
```

```python
from contextlib import ExitStack

import concourse.bass as bass
from concourse import mybir

F32 = mybir.dt.float32
F32R = mybir.dt.float32r
I32 = mybir.dt.int32
ALU = mybir.AluOpType
ACT = mybir.ActivationFunctionType

P = 128
N_FEAT = 32
N_DENSE = 16
HALF = N_FEAT // 2
N_SEL = 10
SEL_ROWS = 1000
SEL_K = 8
SEL_P = SEL_ROWS // SEL_K
K_HALF = SEL_K // 2
N_GATH = N_FEAT - N_SEL
CHUNK = 4
CHUNKS = [(c, min(CHUNK, N_GATH - c)) for c in range(0, N_GATH, CHUNK)]
NC = len(CHUNKS)
SEL_PER_TILE = N_SEL // 2
PAIR = 2 * P
ROW_SLOTS = 4
RAW_SLOTS = 8


def feature_slots(shapes):
    small = [f for f in range(N_FEAT) if shapes[f][0] == SEL_ROWS]
    selected = small[:N_SEL]
    return selected, [f for f in range(N_FEAT) if f not in selected]


def weight_rows(slots):
    def pair(a, b):
        i, j = sorted((slots[a], slots[b]))
        return i * N_FEAT - i * (i + 1) // 2 + j - i - 1

    n_pairs = N_FEAT * (N_FEAT - 1) // 2
    rows = []
    for g in range(HALF):
        for f in range(N_FEAT):
            h = f - HALF
            if f < HALF:
                rows.append(pair(f, g + HALF))
            elif h < g:
                rows.append(pair(f, g + HALF))
            elif h > g:
                rows.append(pair(g, h))
            else:
                rows.append(n_pairs + g)
    return rows


def dlrm_tower(nc, dense, ids, ids_selected, tables_selected, tables_gathered,
               w1, b1, w2, b2, w3, identity, row_numbers, upper_mask, out):
    n_samples = ids.shape[0]
    n_tiles = n_samples // P
    n_loops = (n_tiles - 2) // 4
    h1_n, h2_n = w2.shape
    K1, K2, K3 = w1.shape[0] // P, h1_n // P, h2_n // P
    assert n_tiles == 4 * n_loops + 4 and SEL_PER_TILE == 5 and NC >= 5

    with ExitStack() as ctx:
        def sb(name, shape, dt=F32):
            return ctx.enter_context(nc.sbuf_tensor(name, shape, dt))

        def psum(name, shape, dt=F32):
            return ctx.enter_context(nc.psum_tensor(name, shape, dt))

        def sem(name):
            return ctx.enter_context(nc.semaphore(name))

        rows_T = sb("rows_T", [P, 4, P, N_FEAT])
        table_hi = sb("table_hi", [P, N_SEL, SEL_K, P], F32R)
        table_lo = sb("table_lo", [P, N_SEL, SEL_K, P], F32R)
        gathered = sb("gathered", [P, 2, N_GATH, P])
        onehot = sb("onehot", [P, 2, K_HALF, PAIR], F32R)
        id_rows = sb("id_rows", [P, ROW_SLOTS, PAIR], I32)
        tile_ids = sb("tile_ids", [P, 4, N_GATH], I32)
        dense_sb = sb("dense_sb", [P, n_tiles, N_DENSE])
        ident = sb("ident", [P, P])
        row_no = sb("row_no", [P, SEL_K])
        mask = sb("mask", [P, HALF, HALF], I32)
        pairs = sb("pairs", [P, N_FEAT, N_FEAT])
        w1_sb = sb("w1_sb", [P, K1, h1_n])
        w2_sb = sb("w2_sb", [P, K2, h2_n])
        w3_sb = sb("w3_sb", [P, K3])
        b1_sb = sb("b1_sb", [P, K2])
        b2_sb = sb("b2_sb", [P, K3])
        x0 = sb("x0", [P, K1, P])
        x1 = sb("x1", [P, K2, P])
        x2 = sb("x2", [P, K3, P])
        y_sb = sb("y_sb", [1, 2, P])
        raw_at = rows_T[:, 2:4, :, :].rearrange("p t s f -> p (t s f)")

        def raw(f):
            at = (f % RAW_SLOTS) * SEL_K * P
            return raw_at[0:SEL_P, at:at + SEL_K * P]

        rows_ps = psum("rows_ps", [P, 2, CHUNK, P])
        sel_ps = psum("sel_ps", [P, 2, 2, PAIR])
        gram_ps = psum("gram_ps", [P, P // 4, N_FEAT])
        x01_ps = psum("x01_ps", [P, K1, P])
        x2_ps = psum("x2_ps", [P, 4, P])

        row_no_in = sem("row_no_in")
        consts_in = sem("consts_in")
        weights_in = sem("weights_in")
        table_in = [sem(f"table_in{f}") for f in range(N_SEL)]
        id_row_in = [sem(f"id_row_in{s}") for s in range(ROW_SLOTS)]
        tile_ids_in = [sem(f"tile_ids_in{s}") for s in range(4)]
        chunk_in = [[sem(f"chunk_in{b}_{c}") for c in range(NC)] for b in range(2)]
        hi_ready = sem("hi_ready")
        table_ready = sem("table_ready")
        onehot_ready = sem("onehot_ready")
        onehot_used = sem("onehot_used")
        sel_moved = sem("sel_moved")
        chunk_turned = sem("chunk_turned")
        chunk_moved = sem("chunk_moved")
        gram_done = sem("gram_done")
        gram_read = sem("gram_read")
        pairs_merged = sem("pairs_merged")
        pairs_ready = sem("pairs_ready")
        x0_done = sem("x0_done")
        x0_ready = sem("x0_ready")
        x1_done = sem("x1_done")
        x1_ready = sem("x1_ready")
        x2_done = sem("x2_done")
        x2_ready = sem("x2_ready")
        y_done = sem("y_done")
        y_ready = sem("y_ready")
        out_stored = [sem(f"out_stored{b}") for b in range(2)]

        def count(i, a, per_tile=1, more=0):
            return i * (4 * per_tile) + (per_tile * a + more)

        def selection(i, a, e):
            return 4 * SEL_PER_TILE, N_SEL + SEL_PER_TILE * a + e

        def wait_count(engine, semaphore, value):
            if not isinstance(value, int) or value > 0:
                engine.wait_ge(semaphore, value)

        block = ctx.enter_context(nc.Block())

        @block.sync
        def _(sp):
            def load_id_row(i, q_step, q):
                slot, f, pair = q % ROW_SLOTS, q % N_SEL, q // N_SEL
                if q >= ROW_SLOTS:
                    sp.wait_ge(onehot_ready, i * (2 * q_step) + 2 * (q - ROW_SLOTS + 1))
                column = i * (q_step // N_SEL * PAIR) + pair * PAIR
                sp.dma_start(id_rows[:, slot, :],
                             ids_selected[f:f + 1, bass.ds(column, PAIR)].to_broadcast([P, PAIR])
                             ).then_inc(id_row_in[slot], 16)

            sp.dma_start(row_no[:, :], row_numbers).then_inc(row_no_in, 16)
            sp.dma_start(raw(0), tables_selected[0]).then_inc(table_in[0], 16)
            load_id_row(0, 0, 0)
            load_id_row(0, 0, 1)
            sp.dma_start(raw(1), tables_selected[1]).then_inc(table_in[1], 16)
            sp.dma_start(ident[:, :], identity).then_inc(consts_in, 16)
            sp.dma_start(mask[:, :, :], upper_mask).then_inc(consts_in, 16)
            sp.dma_start(dense_sb[:, :, :], dense.rearrange("(t p) k -> p t k", p=P)).then_inc(consts_in, 16)
            for f in range(2, N_SEL):
                load_id_row(0, 0, f)
                if f >= RAW_SLOTS:
                    sp.wait_ge(table_ready, f - RAW_SLOTS + 1)
                sp.dma_start(raw(f), tables_selected[f]).then_inc(table_in[f], 16)
            for src, dst in ((w1.rearrange("(k p) n -> p k n", p=P), w1_sb[:, :, :]),
                             (w2.rearrange("(k p) n -> p k n", p=P), w2_sb[:, :, :]),
                             (w3, w3_sb[:, :]), (b1, b1_sb[:, :]), (b2, b2_sb[:, :])):
                sp.dma_start(dst, src).then_inc(weights_in, 16)

            def step(i, a):
                for e in range(SEL_PER_TILE):
                    load_id_row(i, *selection(i, a, e))

            step(0, 0)
            step(0, 1)
            with sp.Fori(0, n_loops) as i:
                for a in range(2, 6):
                    step(i, a)
            for stored in out_stored:
                sp.wait_ge(stored, n_tiles // 2 * 16)

        @block.gpsimd
        def _(pool):
            def gather_tile(i, a):
                pool.wait_ge(tile_ids_in[a % 4], i * 16 + 16 * (a // 4 + 1))
                for c, (first, n) in enumerate(CHUNKS):
                    if not (isinstance(i, int) and 4 * i + a < 2):
                        pool.wait_ge(chunk_turned, count(i, a - 2, NC, c + 1))
                    pool.nop(nofuse=True)
                    for g in range(first, first + n):
                        slot_id = tile_ids[:, a % 4, g:g + 1]
                        nc.gpsimd.indirect_dma_start(
                            gathered[:, a % 2, g, :], None, tables_gathered[g],
                            bass.IndirectOffsetOnAxis(ap=slot_id, axis=0)).then_inc(chunk_in[a % 2][c], 16)

            gather_tile(0, 0)
            gather_tile(0, 1)
            with pool.Fori(0, n_loops) as i:
                for a in range(2, 6):
                    gather_tile(i, a)
            gather_tile(n_loops, 2)
            gather_tile(n_loops, 3)

        @block.tensor
        def _(pe):
            def turn_chunk(i, a, c):
                first, n = CHUNKS[c]
                pe.wait_ge(chunk_in[a % 2][c], (i * 2 + (a // 2 + 1)) * (16 * n))
                if not (isinstance(i, int) and NC * (4 * i + a) + c < 2):
                    pe.wait_ge(chunk_moved, count(i, a, NC, c - 1))
                for g in range(n):
                    last = nc.tensor.transpose(rows_ps[:, c % 2, g, :], gathered[:, a % 2, first + g, :],
                                               ident[:, :])
                last.then_inc(chunk_turned, 1)

            def select(i, q_step, q):
                f = q % N_SEL
                for h in range(2):
                    pe.wait_ge(onehot_ready, i * (2 * q_step) + 2 * q + h + 1)
                    if h == 0 and q >= 2:
                        pe.wait_ge(sel_moved, i * q_step + q - 1)
                    for kk in range(K_HALF):
                        k = h * K_HALF + kk
                        for part in (table_hi, table_lo):
                            last = nc.tensor.matmul(sel_ps[:, q % 2, 0, :], part[0:SEL_P, f, k, :],
                                                    onehot[0:SEL_P, h, kk, :],
                                                    start=(k == 0 and part is table_hi),
                                                    stop=(k == SEL_K - 1 and part is table_lo))
                    last.then_inc(onehot_used, 1)

            def gram(i, a):
                pe.wait_ge(chunk_moved, count(i, a, NC, NC))
                pe.wait_ge(sel_moved, (i * 2 + (a // 2 + 1)) * N_SEL)
                wait_count(pe, gram_read, count(i, a))
                for s in range(P // 4):
                    for j in range(4):
                        rows = rows_T[:, a % 4, j * (P // 4) + s, :]
                        last = nc.tensor.matmul(gram_ps[32 * j:32 * j + 32, s, :], rows, rows,
                                                start=True, stop=True)
                last.then_inc(gram_done, 1)

            def turn_pairs(i, a):
                pe.wait_ge(pairs_ready, count(i, a, 1, 1))
                wait_count(pe, x1_ready, count(i, a))
                for k in range(K1):
                    g = HALF + k * (P // N_FEAT)
                    last = nc.tensor.transpose(x01_ps[:, k, :],
                                               pairs[:, g:g + P // N_FEAT, :].rearrange("p g f -> p (g f)"),
                                               ident[:, :])
                last.then_inc(x0_done, 1)

            def layer1(i, a):
                pe.wait_ge(x0_ready, count(i, a, 1, 1))
                for n in range(K2):
                    for k in range(K1):
                        last = nc.tensor.matmul(x01_ps[:, n, :], w1_sb[:, k, n * P:(n + 1) * P], x0[:, k, :],
                                                start=(k == 0), stop=(k == K1 - 1))
                last.then_inc(x1_done, 1)

            def layer2(i, a):
                pe.wait_ge(x1_ready, count(i, a, 1, 1))
                wait_count(pe, y_ready, count(i, a))
                for n in range(K3):
                    for k in range(K2):
                        last = nc.tensor.matmul(x2_ps[:, n, :], w2_sb[:, k, n * P:(n + 1) * P], x1[:, k, :],
                                                start=(k == 0), stop=(k == K2 - 1))
                last.then_inc(x2_done, 1)

            def layer3(i, a):
                pe.wait_ge(x2_ready, count(i, a, 1, 1))
                for k in range(K3):
                    last = nc.tensor.matmul(x2_ps[0:1, K3, :], w3_sb[:, k:k + 1], x2[:, k, :],
                                            start=(k == 0), stop=(k == K3 - 1))
                last.then_inc(y_done, 1)

            def step(i, a, rest=True):
                parts = ([gram], [turn_pairs], [layer1], [layer2], [layer3])
                for n in range(len(parts)):
                    turn_chunk(i, a, n)
                    select(i, *selection(i, a, n))
                    if rest:
                        for part in parts[n]:
                            part(i, a - 1)
                for c in range(len(parts), NC):
                    turn_chunk(i, a, c)

            for f in range(N_SEL):
                pe.wait_ge(table_ready, f + 1)
                select(0, 0, f)
            pe.wait_ge(consts_in, 48)
            step(0, 0, rest=False)
            pe.wait_ge(weights_in, 80)
            step(0, 1)
            with pe.Fori(0, n_loops) as i:
                for a in range(2, 6):
                    step(i, a)
            i = n_loops
            turn_chunk(i, 2, 0)
            turn_chunk(i, 2, 1)
            gram(i, 1)
            for c in range(2, NC):
                turn_chunk(i, 2, c)
            turn_pairs(i, 1)
            gram(i, 2)
            layer1(i, 1)
            turn_chunk(i, 3, 0)
            turn_pairs(i, 2)
            layer2(i, 1)
            turn_chunk(i, 3, 1)
            layer1(i, 2)
            turn_chunk(i, 3, 2)
            layer3(i, 1)
            turn_chunk(i, 3, 3)
            layer2(i, 2)
            turn_chunk(i, 3, 4)
            layer3(i, 2)
            for c in range(5, NC):
                turn_chunk(i, 3, c)
            for part in (gram, turn_pairs, layer1, layer2, layer3):
                part(i, 3)

        @block.scalar
        def _(act):
            def load_tile_ids(i, a):
                act.dma_start(tile_ids[:, a % 4, :], ids[bass.ds(count(i, a, P), P), :]
                              ).then_inc(tile_ids_in[a % 4], 16)

            def move_chunk(i, a, c):
                first, n = CHUNKS[c]
                act.wait_ge(chunk_turned, count(i, a, NC, c + 1))
                nc.scalar.activation(
                    rows_T[:, a % 4, :, N_SEL + first:N_SEL + first + n],
                    rows_ps[:, c % 2, 0:n, :].rearrange("p f s -> p s f"), ACT.Copy).then_inc(chunk_moved, 1)

            def move_selection(i, q_step, q, pair_place):
                act.wait_ge(onehot_used, i * (2 * q_step) + 2 * q + 2)
                nc.scalar.activation(
                    rows_T[:, 2 * pair_place:2 * pair_place + 2, :, q % N_SEL].rearrange("p t s -> p (t s)"),
                    sel_ps[:, q % 2, 0, :], ACT.Copy).then_inc(sel_moved, 1)

            def move_x0(i, a):
                act.wait_ge(x0_done, count(i, a, 1, 1))
                wait_count(act, x1_done, count(i, a))
                nc.scalar.activation(x0[:, :, :], x01_ps[:, :, :], ACT.Copy).then_inc(x0_ready, 1)

            def move_x1(i, a):
                act.wait_ge(x1_done, count(i, a, 1, 1))
                wait_count(act, x2_done, count(i, a))
                for n in range(K2):
                    last = nc.scalar.activation(x1[:, n, :], x01_ps[:, n, :], ACT.Relu, bias=b1_sb[:, n:n + 1])
                last.then_inc(x1_ready, 1)

            def move_x2(i, a):
                act.wait_ge(x2_done, count(i, a, 1, 1))
                wait_count(act, y_done, count(i, a))
                for n in range(K3):
                    last = nc.scalar.activation(x2[:, n, :], x2_ps[:, n, :], ACT.Relu, bias=b2_sb[:, n:n + 1])
                last.then_inc(x2_ready, 1)

            def move_y(i, a):
                act.wait_ge(y_done, count(i, a, 1, 1))
                wait_count(act, out_stored[a % 2], i * 32 + a // 2 * 16)
                nc.scalar.activation(y_sb[:, a % 2, :], x2_ps[0:1, K3, :], ACT.Copy).then_inc(y_ready, 1)
                act.wait_ge(y_ready, count(i, a, 1, 1))
                act.dma_start(out[:, bass.ds(count(i, a, P), P)], y_sb[:, a % 2, :]
                              ).then_inc(out_stored[a % 2], 16)

            def step(i, a, rest=True, ids_ahead=()):
                for ahead in ids_ahead:
                    load_tile_ids(i, ahead)
                parts = ([], [move_x0], [move_x1], [move_x2], [move_y])
                for n in range(len(parts)):
                    move_chunk(i, a, n)
                    if n == 0 and a % 2 == 0 and rest:
                        wait_count(act, gram_done, count(i, a))
                    move_selection(i, *selection(i, a, n), (a // 2 + 1) % 2)
                    if rest:
                        for part in parts[n]:
                            part(i, a - 1)
                for c in range(len(parts), NC):
                    move_chunk(i, a, c)

            for t in range(4):
                load_tile_ids(0, t)
            for f in range(N_SEL):
                act.wait_ge(table_in[f], 16)
                nc.scalar.activation(table_hi[0:SEL_P, f, :, :].rearrange("p k d -> p (k d)"), raw(f),
                                     ACT.Copy).then_inc(hi_ready, 1)
                if f >= 2:
                    move_selection(0, 0, f - 2, 0)
            move_selection(0, 0, N_SEL - 2, 0)
            move_selection(0, 0, N_SEL - 1, 0)
            step(0, 0, rest=False)
            act.wait_ge(weights_in, 80)
            step(0, 1)
            with act.Fori(0, n_loops) as i:
                for a, ids_ahead in ((2, (4, 5)), (3, (6,)), (4, (7,)), (5, ())):
                    step(i, a, ids_ahead=ids_ahead)
            i = n_loops
            for c in range(NC):
                move_chunk(i, 2, c)
            move_x0(i, 1)
            move_x1(i, 1)
            move_chunk(i, 3, 0)
            move_x0(i, 2)
            move_x2(i, 1)
            move_chunk(i, 3, 1)
            move_x1(i, 2)
            move_chunk(i, 3, 2)
            move_y(i, 1)
            move_chunk(i, 3, 3)
            move_x2(i, 2)
            move_chunk(i, 3, 4)
            move_y(i, 2)
            for c in range(5, NC):
                move_chunk(i, 3, c)
            for part in (move_x0, move_x1, move_x2, move_y):
                part(i, 3)

        @block.vector
        def _(dve):
            def compare(i, q_step, q):
                slot = q % ROW_SLOTS
                dve.wait_ge(id_row_in[slot], i * (q_step // ROW_SLOTS * 16) + 16 * (q // ROW_SLOTS + 1))
                for h in range(2):
                    if q >= 1:
                        dve.wait_ge(onehot_used, i * (2 * q_step) + 2 * q + h - 1)
                    for kk in range(K_HALF):
                        k = h * K_HALF + kk
                        last = nc.vector.tensor_scalar(onehot[:, h, kk, :], id_rows[:, slot, :],
                                                       row_no[:, k:k + 1], None, ALU.is_equal)
                    last.then_inc(onehot_ready, 1)

            def pack_pairs(i, a):
                dve.wait_ge(gram_done, count(i, a, 1, 1))
                wait_count(dve, x0_done, count(i, a))
                nc.vector.transpose(pairs[:, :, :], gram_ps[:, :, :].rearrange("p s g -> p g s")
                                    ).then_inc(gram_read, 1)
                dve.wait_ge(gram_read, count(i, a, 1, 1))
                dve.nop(nofuse=True)
                nc.vector.copy_predicated(pairs[:, HALF:, HALF:], mask[:, :, :], pairs[:, 0:HALF, 0:HALF]
                                          ).then_inc(pairs_merged, 1)
                dve.wait_ge(pairs_merged, count(i, a, 1, 1))
                diagonal = pairs[:, HALF:, :].rearrange("p g f -> p (g f)")[:, HALF::N_FEAT + 1]
                nc.vector.tensor_copy(diagonal, dense_sb[:, bass.ds(count(i, a), 1), :].rearrange(
                    "p t k -> p (t k)")).then_inc(pairs_ready, 1)

            def step(i, a, rest=True):
                for n in range(2):
                    compare(i, *selection(i, a, n))
                if rest:
                    pack_pairs(i, a - 1)
                for n in range(2, SEL_PER_TILE):
                    compare(i, *selection(i, a, n))

            dve.wait_ge(row_no_in, 16)
            for f in range(N_SEL):
                dve.wait_ge(hi_ready, f + 1)
                nc.vector.tensor_tensor(table_lo[0:SEL_P, f, :, :].rearrange("p k d -> p (k d)"), raw(f),
                                        table_hi[0:SEL_P, f, :, :].rearrange("p k d -> p (k d)").bitcast(F32),
                                        ALU.subtract).then_inc(table_ready, 1)
                compare(0, 0, f)
            dve.wait_ge(consts_in, 48)
            step(0, 0, rest=False)
            step(0, 1)
            with dve.Fori(0, n_loops) as i:
                for a in range(2, 6):
                    step(i, a)
            for a in range(1, 4):
                pack_pairs(n_loops, a)


def kernel(**inputs):
    import numpy as np
    import concourse.bacc as bacc
    from concourse.bass_utils import run_bass_kernel_spmd

    tables = [np.asarray(inputs[f"tbl_{f}"]) for f in range(N_FEAT)]
    selected, gathered = feature_slots([t.shape for t in tables])
    ids = np.asarray(inputs["ids"])
    arrays = {
        "dense": np.asarray(inputs["dense_ctx"]),
        "ids": ids[:, gathered],
        "ids_selected": ids[:, selected].T,
        "tables_selected": np.stack([tables[f].reshape(SEL_P, SEL_K * P) for f in selected]),
        **{f"table_{f}": tables[f] for f in gathered},
        "w1": np.asarray(inputs["W_top1"])[weight_rows(selected + gathered)],
        "b1": np.asarray(inputs["b_top1"]).reshape(-1, P).T,
        "w2": np.asarray(inputs["W_top2"]),
        "b2": np.asarray(inputs["b_top2"]).reshape(-1, P).T,
        "w3": np.asarray(inputs["W_top3"]).reshape(-1, P).T,
        "identity": np.eye(P, dtype=np.float32),
        "row_numbers": np.arange(P * SEL_K, dtype=np.float32).reshape(P, SEL_K),
        "upper_mask": np.tile(np.triu(np.ones((HALF, HALF), np.int32), 1), (P, 1, 1)),
    }
    arrays = {name: np.ascontiguousarray(a) for name, a in arrays.items()}
    nc = bacc.Bacc("TRN2", target_bir_lowering=False, num_devices=1)
    dram = {name: nc.dram_tensor(name, a.shape, mybir.dt.from_np(a.dtype), kind="ExternalInput").ap()
            for name, a in arrays.items()}
    n_samples = ids.shape[0]
    out = nc.dram_tensor("out", (1, n_samples), F32, kind="ExternalOutput").ap()
    dlrm_tower(nc, dram["dense"], dram["ids"], dram["ids_selected"], dram["tables_selected"],
               [dram[f"table_{f}"] for f in gathered], dram["w1"], dram["b1"], dram["w2"], dram["b2"],
               dram["w3"], dram["identity"], dram["row_numbers"], dram["upper_mask"], out)
    result = run_bass_kernel_spmd(nc, [arrays], core_ids=[0])
    return result.results[0]["out"].reshape(n_samples, 1)
```
